# Optimizing a Trainium2 kernel written in Bass

```python
import numpy as np
import jax
import jax.numpy as jnp

def _softmax(x, axis=-1):
    return jax.nn.softmax(x, axis=axis)

def _gelu(x):
    return jax.nn.gelu(x, approximate=True)

def _silu(x):
    return jax.nn.silu(x)

def _sigmoid(x):
    return jax.nn.sigmoid(x)

def _layernorm(x, axis=-1, eps=1e-05):
    m = jnp.mean(x, axis=axis, keepdims=True)
    v = jnp.var(x, axis=axis, keepdims=True)
    return (x - m) / jnp.sqrt(v + eps)

def _scatter_add(tgt, idx, src, axis=0):
    return tgt.at[idx].add(src)

def _segment_sum(src, seg, n):
    return jax.ops.segment_sum(src, seg, n)
kernel_name = 'mk_adaln_ffn_d1_seqx_r4_237bf5'

def setup_inputs(seed: int=0):
    np.random.seed(seed)
    _w = jnp.asarray

    def _rec_inputs():
        import jax
        import jax.numpy as jnp
        _rk = jax.random.key(seed)
        x = -7.109e-05 + 0.9999 * jax.random.normal(jax.random.fold_in(_rk, 1), (128, 64, 1024), jnp.float32)
        _lenS = 64 - jax.random.randint(jax.random.fold_in(_rk, 7), (128,), 0, max(1, 64 // 4) + 1, jnp.int32)
        _lenS2 = 64 - jax.random.randint(jax.random.fold_in(_rk, 8), (128,), 0, max(1, 64 // 4) + 1, jnp.int32)
        itok_B_0_15 = jax.random.randint(jax.random.fold_in(_rk, 11), (128,), 0, 16, jnp.int32)
        return (x, itok_B_0_15)
    x, itok_B_0_15 = _rec_inputs()

    def _L0_cond_setup():
        import jax, jax.numpy as jnp
        import numpy as np
        B, C, T = (64, 64, 1024)
        S, D = (16, 64)
        key = jax.random.key(seed)
        k1, k2, k3 = jax.random.split(key, 3)
        x = jax.random.normal(k1, (B, C, T), dtype=jnp.float32)
        condition = jax.random.randint(k2, (B,), 0, S, dtype=jnp.int64)
        bound = float(np.sqrt(6.0 / C))
        weights = jax.random.uniform(k3, (S, C, D), dtype=jnp.float32, minval=-bound, maxval=bound)
        return {'x': x, 'condition': condition, 'weights': weights}
    _L0_cond_all = _L0_cond_setup()
    _L0_cond_in = {k: v for k, v in _L0_cond_all.items() if k in ('weights',)}
    del _L0_cond_all

    def _L0_ffn_setup():
        import jax, jax.numpy as jnp
        import numpy as np
        B, S, IN, OUT = (4, 512, 1024, 1024)
        key = jax.random.key(seed)
        k_x, k_w, k_s, k_b = jax.random.split(key, 4)
        x = jax.random.normal(k_x, (B, S, IN), dtype=jnp.float16)
        w_q = jax.random.randint(k_w, (IN, OUT), -128, 128, dtype=jnp.int32).astype(jnp.int8)
        scale = (jax.random.uniform(k_s, (OUT,), dtype=jnp.float32) * 0.02 + 0.001).astype(jnp.float16)
        bias = jax.random.normal(k_b, (OUT,), dtype=jnp.float16)
        return {'x': x, 'w_q': w_q, 'scale': scale, 'bias': bias}
    _L0_ffn_all = _L0_ffn_setup()
    _L0_ffn_in = {k: v for k, v in _L0_ffn_all.items() if k in ('w_q', 'scale', 'bias')}
    del _L0_ffn_all
    return {'x': x, 'itok_B_0_15': itok_B_0_15, 'L0_cond_weights': _L0_cond_in['weights'], 'L0_ffn_w_q': _L0_ffn_in['w_q'], 'L0_ffn_scale': _L0_ffn_in['scale'], 'L0_ffn_bias': _L0_ffn_in['bias']}

def reference(x, itok_B_0_15, L0_cond_weights, L0_ffn_w_q, L0_ffn_scale, L0_ffn_bias):
    import jax
    import jax.numpy as jnp

    def _L0_cond_ref(x, condition, weights):
        import jax, jax.numpy as jnp
        import numpy as np
        B, C, T = (64, 64, 1024)
        S, D = (16, 64)
        W = weights[condition]
        return jnp.einsum('bct,bcd->bdt', x, W)

    def _L0_ffn_ref(x, w_q, scale, bias):
        import jax, jax.numpy as jnp
        import numpy as np
        B, S, IN, OUT = (4, 512, 1024, 1024)
        w = w_q.astype(jnp.float16) * scale[None, :]
        out = jnp.einsum('bsi,io->bso', x, w)
        return out + bias
    x = x + _L0_ffn_ref(_L0_cond_ref(x, itok_B_0_15, L0_cond_weights), L0_ffn_w_q, L0_ffn_scale, L0_ffn_bias)
    return x

_drawn_inputs = setup_inputs


def setup_inputs(seed=0):
    import zlib

    import numpy as np

    out = dict(_drawn_inputs(seed))
    spreads = {}
    factors = {}
    for name, (base, spread) in spreads.items():
        noise = np.random.default_rng([zlib.crc32(name.encode()), seed]).standard_normal(out[name].shape)
        drawn = base * np.exp(spread * noise) if base else spread * noise
        out[name] = jnp.asarray(drawn.astype(out[name].dtype))
    for name, factor in factors.items():
        out[name] = (out[name] * factor).astype(out[name].dtype)
    return out
```

```python
import concourse.bass as bass
from concourse import mybir
from contextlib import ExitStack


def cond_ffn_residual(
    nc: bass.Bass,
    x: bass.AP,
    cond: bass.AP,
    cond_w: bass.AP,
    w_q_words: bass.AP,
    scale: bass.AP,
    bias: bass.AP,
    out: bass.AP,
):
    fp32 = mybir.dt.float32
    fp32r = mybir.dt.float32r
    fp16 = mybir.dt.float16
    int8 = mybir.dt.int8
    int32 = mybir.dt.int32
    ALU = mybir.AluOpType
    ACT = mybir.ActivationFunctionType

    P = 128
    B, C, T = x.shape
    S, _, D = cond_w.shape
    O = bias.shape[0]
    BP = P // C
    PAIRS = B // BP
    KT = T // P
    NH = 512
    HALVES = O // NH
    SLOTS = 4
    ROUNDS = PAIRS // SLOTS
    YS = 2
    DMA = 16

    x_pairs = x.rearrange("(n b) c t -> n (b c) t", b=BP)
    out_pairs = out.rearrange("(n b) d o -> n (b d) o", b=BP)
    cond_w_rows = cond_w.rearrange("s c d -> (s c) d")

    ctx = ExitStack()
    with ctx:
        def sb(name, shape, dt):
            return ctx.enter_context(nc.sbuf_tensor(name, shape, dt))

        def pb(name, shape, dt):
            return ctx.enter_context(nc.psum_tensor(name, shape, dt))

        def sem(name):
            return ctx.enter_context(nc.semaphore(name))

        cond_sb = sb("cond_sb", [1, B], int32)
        wq_words = sb("wq_words", [P, KT, O // 4], int32)
        wq_sb = wq_words[:, :, :].bitcast(int8)
        wq16 = sb("wq16", [P, KT, O], fp16)
        w16 = sb("w16", [P, KT, O], fp16)
        w = sb("w", [P, KT, O], fp32r)
        scale_bc = sb("scale_bc", [P, O], fp16)
        bias_bc = sb("bias_bc", [P, O], fp16)
        xs = [sb(f"xs{s}", [P, T], fp32) for s in range(SLOTS)]
        cw = [sb(f"cw{s}", [P, D], fp32) for s in range(SLOTS)]
        res = [sb(f"res{s}", [P, O], fp32) for s in range(SLOTS)]
        y_hi = [sb(f"y_hi{s}", [P, KT, BP, D], fp32r) for s in range(YS)]
        y_lo = [sb(f"y_lo{s}", [P, KT, BP, D], fp32r) for s in range(YS)]
        y_ps = [pb(f"y_ps{b}", [P, KT, D], fp32) for b in range(BP)]
        z_ps = [[pb(f"z_ps{s}_{h}", [P, NH], fp32) for h in range(HALVES)] for s in range(YS)]

        s_cond = sem("cond_loaded")
        s_scale = sem("scale_loaded")
        s_bias = sem("bias_loaded")
        s_wq = [sem(f"wq_loaded{k}") for k in range(KT)]
        s_wq16 = sem("wq16_ready")
        s_w16 = sem("w16_ready")
        s_w = sem("w_ready")
        s_x = [sem(f"x_loaded{s}") for s in range(SLOTS)]
        s_cw = [sem(f"cw_loaded{s}") for s in range(SLOTS)]
        s_y = sem("y_done")
        s_yhi = sem("y_hi_ready")
        s_ylo = sem("y_lo_ready")
        s_z = sem("z_half_done")
        s_xb = sem("x_plus_bias_ready")
        s_res = sem("result_half_ready")
        s_out = [sem(f"out_stored{s}") for s in range(SLOTS)]

        block = ctx.enter_context(nc.Block())

        def rounds(eng, body):
            body(0, True, False)
            with eng.Fori(1, ROUNDS - 1) as r:
                body(r, False, False)
            body(ROUNDS - 1, False, True)

        @block.sync
        def _(sp):
            sp.dma_start(cond_sb[:, :], cond.rearrange("(a b) -> a b", a=1)).then_inc(s_cond, DMA)

            def load(pair, s):
                sp.dma_start(xs[s][:, :], x_pairs[bass.ds(pair, 1), :, :].rearrange("a p t -> (a p) t")
                             ).then_inc(s_x[s], DMA)
                for b in range(BP):
                    c = sp.value_load(cond_sb[0:1, bass.ds(pair * BP + b, 1)], min_val=0, max_val=S - 1)
                    sp.dma_start(cw[s][b * C:(b + 1) * C, :],
                                 cond_w_rows[bass.ds(c * C, C), :]).then_inc(s_cw[s], DMA)

            sp.dma_start(xs[0][:, :], x_pairs[0, :, :]).then_inc(s_x[0], DMA)
            sp.wait_ge(s_cond, DMA)
            for b in range(BP):
                c = sp.value_load(cond_sb[0:1, b:b + 1], min_val=0, max_val=S - 1)
                sp.dma_start(cw[0][b * C:(b + 1) * C, :],
                             cond_w_rows[bass.ds(c * C, C), :]).then_inc(s_cw[0], DMA)
            for s in range(1, SLOTS):
                load(s, s)

            def body(r, first, last):
                for s in range(SLOTS):
                    pair = r * SLOTS + s
                    if not last:
                        sp.wait_ge(s_y, pair + 1)
                        sp.wait_ge(s_xb, pair + 1)
                        load(pair + SLOTS, s)
                    sp.wait_ge(s_res, HALVES * (pair + 1))
                    sp.dma_start(out_pairs[bass.ds(pair, 1), :, :].rearrange("a p o -> (a p) o"),
                                 res[s][:, :]).then_inc(s_out[s], DMA)

            rounds(sp, body)
            for s in range(SLOTS):
                sp.wait_ge(s_out[s], DMA * ROUNDS)

        @block.gpsimd
        def _(pool):
            pool.wait_ge(s_bias, DMA)

            def body(r, first, last):
                for s in range(SLOTS):
                    pair = r * SLOTS + s
                    pool.wait_ge(s_x[s], DMA * (r + 1))
                    if not first:
                        pool.wait_ge(s_out[s], DMA * r)
                    nc.gpsimd.tensor_tensor(res[s][:, :], xs[s][:, :], bias_bc[:, :], ALU.add
                                            ).then_inc(s_xb, 1)

            rounds(pool, body)

        @block.scalar
        def _(act):
            act.dma_start(scale_bc[:, :], scale.rearrange("(a o) -> a o", a=1).to_broadcast([P, O])
                          ).then_inc(s_scale, DMA)
            for k in range(KT):
                act.dma_start(wq_words[:, k, :], w_q_words[k * P:(k + 1) * P, :]).then_inc(s_wq[k], DMA)
            act.dma_start(bias_bc[:, :], bias.rearrange("(a o) -> a o", a=1).to_broadcast([P, O])
                          ).then_inc(s_bias, DMA)
            for k in range(KT):
                act.wait_ge(s_wq[k], DMA)
                nc.scalar.activation(wq16[:, k, :], wq_sb[:, k, :], ACT.Copy).then_inc(s_wq16, 1)

            def body(r, first, last):
                for s in range(SLOTS):
                    pair = r * SLOTS + s
                    act.wait_ge(s_y, pair + 1)
                    if not first or s >= YS:
                        act.wait_ge(s_z, HALVES * (pair - YS + 1))
                    for b in range(BP):
                        nc.scalar.activation(y_hi[s % YS][:, :, b, :], y_ps[b][:, :, :], ACT.Copy
                                             ).then_inc(s_yhi, 1)

            rounds(act, body)

        @block.vector
        def _(dve):
            dve.wait_ge(s_scale, DMA)
            for k in range(KT):
                dve.wait_ge(s_wq16, k + 1)
                nc.vector.tensor_tensor(w16[:, k, :], wq16[:, k, :], scale_bc[:, :], ALU.mult
                                        ).then_inc(s_w16, 1)
                dve.wait_ge(s_w16, k + 1)
                nc.vector.tensor_copy(w[:, k, :], w16[:, k, :]).then_inc(s_w, 1)

            def split(pair, s, first):
                if not (first and s < YS):
                    dve.wait_ge(s_z, HALVES * (pair - YS + 1))
                for b in range(BP):
                    dve.wait_ge(s_yhi, BP * pair + b + 1)
                    nc.vector.tensor_tensor(y_lo[s % YS][:, :, b, :], y_ps[b][:, :, :],
                                            y_hi[s % YS][:, :, b, :].bitcast(fp32), ALU.subtract
                                            ).then_inc(s_ylo, 1)

            split(0, 0, True)

            def body(r, first, last):
                for s in range(SLOTS):
                    pair = r * SLOTS + s
                    if not (last and s == SLOTS - 1):
                        split(pair + 1, (s + 1) % SLOTS, first and s < SLOTS - 1)
                    dve.wait_ge(s_xb, pair + 1)
                    for h in range(HALVES):
                        dve.wait_ge(s_z, HALVES * pair + h + 1)
                        nc.vector.tensor_tensor(res[s][:, h * NH:(h + 1) * NH], z_ps[s % YS][h][:, :],
                                                res[s][:, h * NH:(h + 1) * NH], ALU.add
                                                ).then_inc(s_res, 1)

            rounds(dve, body)

        @block.tensor
        def _(pe):
            def stage1(pair, s, r, first):
                pe.wait_ge(s_x[s], DMA * (r + 1))
                pe.wait_ge(s_cw[s], BP * DMA * (r + 1))
                if not first:
                    pe.wait_ge(s_ylo, BP * pair)
                for k in range(KT):
                    for b in range(BP):
                        c = slice(b * C, (b + 1) * C)
                        last = nc.tensor.matmul(y_ps[b][:, k, :], xs[s][c, k * P:(k + 1) * P], cw[s][c, :],
                                                start=True, stop=True)
                last.then_inc(s_y, 1)

            def stage2(pair, s, first, first_pair):
                pe.wait_ge(s_yhi, BP * (pair + 1))
                pe.wait_ge(s_ylo, BP * (pair + 1))
                if not (first and s < YS):
                    pe.wait_ge(s_res, HALVES * (pair - YS + 1))
                for h in range(HALVES):
                    for k in range(KT):
                        if first_pair and h == 0:
                            pe.wait_ge(s_w, k + 1)
                        for part in (y_hi, y_lo):
                            last = nc.tensor.matmul(z_ps[s % YS][h][:, :],
                                                    part[s % YS][:, k, :, :].rearrange("p b d -> p (b d)"),
                                                    w[:, k, h * NH:(h + 1) * NH],
                                                    start=(k == 0 and part is y_hi),
                                                    stop=(k == KT - 1 and part is y_lo))
                    last.then_inc(s_z, 1)

            stage1(0, 0, 0, True)

            def body(r, first, last):
                for s in range(SLOTS):
                    pair = r * SLOTS + s
                    if not (last and s == SLOTS - 1):
                        stage1(pair + 1, (s + 1) % SLOTS, r + (s + 1) // SLOTS, False)
                    stage2(pair, s, first, first and s == 0)

            rounds(pe, body)


_INS = ['x', 'itok_B_0_15', 'L0_cond_weights', 'L0_ffn_w_q', 'L0_ffn_scale', 'L0_ffn_bias']
_OUTS = [((128, 64, 1024), 'float32')]


def kernel(**inputs):
    import numpy as _np
    import concourse.bacc as _bacc
    from concourse import mybir as _mybir
    from concourse.bass_utils import run_bass_kernel_spmd as _run

    nc = _bacc.Bacc("TRN2", target_bir_lowering=False, num_devices=1)
    arrays, args = {}, []
    for name in _INS:
        a = _np.ascontiguousarray(inputs[name])
        if a.dtype == _np.int8:
            a = a.view(_np.int32)
        arrays[f"in_{name}_dram"] = a
        args.append(nc.dram_tensor(f"in_{name}_dram", a.shape, _mybir.dt.from_np(a.dtype), kind="ExternalInput").ap())
    for i, (shape, dtype) in enumerate(_OUTS):
        dt = _mybir.dt.from_np(_np.dtype(dtype))
        args.append(nc.dram_tensor(f"out_{i}_dram", shape, dt, kind="ExternalOutput").ap())
    cond_ffn_residual(nc, *args)
    r = _run(nc, [arrays], core_ids=[0])
    got = tuple(r.results[0][f"out_{i}_dram"] for i in range(len(_OUTS)))
    return got[0]
```

```python
import concourse.bass as bass
from concourse import mybir
from contextlib import ExitStack


def cond_ffn_residual(
    nc: bass.Bass,
    x: bass.AP,
    cond: bass.AP,
    cond_w: bass.AP,
    w_q_words: bass.AP,
    scale: bass.AP,
    bias: bass.AP,
    out: bass.AP,
):
    fp32 = mybir.dt.float32
    fp32r = mybir.dt.float32r
    fp16 = mybir.dt.float16
    int8 = mybir.dt.int8
    int32 = mybir.dt.int32
    ALU = mybir.AluOpType
    ACT = mybir.ActivationFunctionType

    P = 128
    B, C, T = x.shape
    S, _, D = cond_w.shape
    O = bias.shape[0]
    BP = P // C
    PAIRS = B // BP
    KT = T // P
    NH = 512
    HALVES = O // NH
    KQ = NH // P
    YB = KT // KQ
    SLOTS = 4
    ROUNDS = PAIRS // SLOTS
    YS = 2
    DMA = 16

    x_pairs = x.rearrange("(n b) c t -> n (b c) t", b=BP)
    out_pairs = out.rearrange("(n b) d o -> n (b d) o", b=BP)
    cond_w_rows = cond_w.rearrange("s c d -> (s c) d")

    ctx = ExitStack()
    with ctx:
        def sb(name, shape, dt):
            return ctx.enter_context(nc.sbuf_tensor(name, shape, dt))

        def pb(name, shape, dt):
            return ctx.enter_context(nc.psum_tensor(name, shape, dt))

        def sem(name):
            return ctx.enter_context(nc.semaphore(name))

        cond_sb = sb("cond_sb", [1, B], int32)
        wq_words = sb("wq_words", [P, KT, O // 4], int32)
        wq_sb = wq_words[:, :, :].bitcast(int8)
        wq16 = sb("wq16", [P, KT, O], fp16)
        w16 = sb("w16", [P, KT, O], fp16)
        w = sb("w", [P, KT, O], fp32r)
        scale_bc = sb("scale_bc", [P, O], fp16)
        bias_bc = sb("bias_bc", [P, O], fp16)
        xs = [sb(f"xs{s}", [P, T], fp32) for s in range(SLOTS)]
        cw = [sb(f"cw{s}", [P, BP * D], fp32) for s in range(SLOTS)]
        res = [sb(f"res{s}", [P, O], fp32) for s in range(SLOTS)]
        y_hi = [sb(f"y_hi{s}", [P, KT, P], fp32r) for s in range(YS)]
        y_lo = [sb(f"y_lo{s}", [P, KT, P], fp32r) for s in range(YS)]
        y_ps = [pb(f"y_ps{q}", [P, KQ, P], fp32) for q in range(YB)]
        z_ps = [[pb(f"z_ps{s}_{h}", [P, NH], fp32) for h in range(HALVES)] for s in range(YS)]

        s_cond = sem("cond_loaded")
        s_scale = sem("scale_loaded")
        s_bias = sem("bias_loaded")
        s_wq = [sem(f"wq_loaded{k}") for k in range(KT)]
        s_wq16 = sem("wq16_ready")
        s_w16 = sem("w16_ready")
        s_w = sem("w_ready")
        s_x = [sem(f"x_loaded{s}") for s in range(SLOTS)]
        s_cw = [sem(f"cw_loaded{s}") for s in range(SLOTS)]
        s_zero = sem("cw_zeroed")
        s_y = sem("y_bank_done")
        s_yhi = sem("y_hi_ready")
        s_ylo = sem("y_lo_ready")
        s_z = sem("z_half_done")
        s_xb = sem("x_plus_bias_ready")
        s_res = sem("result_half_ready")
        s_out = [sem(f"out_stored{s}") for s in range(SLOTS)]

        block = ctx.enter_context(nc.Block())

        def rounds(eng, body):
            body(0, True, False)
            with eng.Fori(1, ROUNDS - 1) as r:
                body(r, False, False)
            body(ROUNDS - 1, False, True)

        @block.sync
        def _(sp):
            sp.dma_start(cond_sb[:, :], cond.rearrange("(a b) -> a b", a=1)).then_inc(s_cond, DMA)

            def load(pair, s):
                sp.dma_start(xs[s][:, :], x_pairs[bass.ds(pair, 1), :, :].rearrange("a p t -> (a p) t")
                             ).then_inc(s_x[s], DMA)
                for b in range(BP):
                    c = sp.value_load(cond_sb[0:1, bass.ds(pair * BP + b, 1)], min_val=0, max_val=S - 1)
                    sp.dma_start(cw[s][b * C:(b + 1) * C, b * D:(b + 1) * D],
                                 cond_w_rows[bass.ds(c * C, C), :]).then_inc(s_cw[s], DMA)

            sp.dma_start(xs[0][:, :], x_pairs[0, :, :]).then_inc(s_x[0], DMA)
            sp.wait_ge(s_cond, DMA)
            sp.wait_ge(s_zero, SLOTS)
            for b in range(BP):
                c = sp.value_load(cond_sb[0:1, b:b + 1], min_val=0, max_val=S - 1)
                sp.dma_start(cw[0][b * C:(b + 1) * C, b * D:(b + 1) * D],
                             cond_w_rows[bass.ds(c * C, C), :]).then_inc(s_cw[0], DMA)
            for s in range(1, SLOTS):
                load(s, s)

            def body(r, first, last):
                for s in range(SLOTS):
                    pair = r * SLOTS + s
                    if not last:
                        sp.wait_ge(s_y, YB * (pair + 1))
                        sp.wait_ge(s_xb, pair + 1)
                        load(pair + SLOTS, s)
                    sp.wait_ge(s_res, HALVES * (pair + 1))
                    sp.dma_start(out_pairs[bass.ds(pair, 1), :, :].rearrange("a p o -> (a p) o"),
                                 res[s][:, :]).then_inc(s_out[s], DMA)

            rounds(sp, body)
            for s in range(SLOTS):
                sp.wait_ge(s_out[s], DMA * ROUNDS)

        @block.gpsimd
        def _(pool):
            pool.wait_ge(s_bias, DMA)

            def body(r, first, last):
                for s in range(SLOTS):
                    pair = r * SLOTS + s
                    pool.wait_ge(s_x[s], DMA * (r + 1))
                    if not first:
                        pool.wait_ge(s_out[s], DMA * r)
                    nc.gpsimd.tensor_tensor(res[s][:, :], xs[s][:, :], bias_bc[:, :], ALU.add
                                            ).then_inc(s_xb, 1)

            rounds(pool, body)

        @block.scalar
        def _(act):
            act.dma_start(scale_bc[:, :], scale.rearrange("(a o) -> a o", a=1).to_broadcast([P, O])
                          ).then_inc(s_scale, DMA)
            for k in range(KT):
                act.dma_start(wq_words[:, k, :], w_q_words[k * P:(k + 1) * P, :]).then_inc(s_wq[k], DMA)
            act.dma_start(bias_bc[:, :], bias.rearrange("(a o) -> a o", a=1).to_broadcast([P, O])
                          ).then_inc(s_bias, DMA)
            for k in range(KT):
                act.wait_ge(s_wq[k], DMA)
                nc.scalar.activation(wq16[:, k, :], wq_sb[:, k, :], ACT.Copy).then_inc(s_wq16, 1)

            def body(r, first, last):
                for s in range(SLOTS):
                    pair = r * SLOTS + s
                    if not first or s >= YS:
                        act.wait_ge(s_z, HALVES * (pair - YS + 1))
                    for q in range(YB):
                        act.wait_ge(s_y, YB * pair + q + 1)
                        nc.scalar.activation(y_hi[s % YS][:, q * KQ:(q + 1) * KQ, :], y_ps[q][:, :, :], ACT.Copy
                                             ).then_inc(s_yhi, 1)

            rounds(act, body)

        @block.vector
        def _(dve):
            for s in range(SLOTS):
                nc.vector.memset(cw[s][:, :], 0.0).then_inc(s_zero, 1)
            dve.wait_ge(s_scale, DMA)
            for k in range(KT):
                dve.wait_ge(s_wq16, k + 1)
                nc.vector.tensor_tensor(w16[:, k, :], wq16[:, k, :], scale_bc[:, :], ALU.mult
                                        ).then_inc(s_w16, 1)
                dve.wait_ge(s_w16, k + 1)
                nc.vector.tensor_copy(w[:, k, :], w16[:, k, :]).then_inc(s_w, 1)

            def split(pair, s, first):
                if not (first and s < YS):
                    dve.wait_ge(s_z, HALVES * (pair - YS + 1))
                for q in range(YB):
                    dve.wait_ge(s_yhi, YB * pair + q + 1)
                    ks = slice(q * KQ, (q + 1) * KQ)
                    nc.vector.tensor_tensor(y_lo[s % YS][:, ks, :], y_ps[q][:, :, :],
                                            y_hi[s % YS][:, ks, :].bitcast(fp32), ALU.subtract
                                            ).then_inc(s_ylo, 1)

            split(0, 0, True)

            def body(r, first, last):
                for s in range(SLOTS):
                    pair = r * SLOTS + s
                    if not (last and s == SLOTS - 1):
                        split(pair + 1, (s + 1) % SLOTS, first and s < SLOTS - 1)
                    dve.wait_ge(s_xb, pair + 1)
                    for h in range(HALVES):
                        dve.wait_ge(s_z, HALVES * pair + h + 1)
                        nc.vector.tensor_tensor(res[s][:, h * NH:(h + 1) * NH], z_ps[s % YS][h][:, :],
                                                res[s][:, h * NH:(h + 1) * NH], ALU.add
                                                ).then_inc(s_res, 1)

            rounds(dve, body)

        @block.tensor
        def _(pe):
            def stage1(pair, s, r, first):
                pe.wait_ge(s_x[s], DMA * (r + 1))
                pe.wait_ge(s_cw[s], BP * DMA * (r + 1))
                if not first:
                    pe.wait_ge(s_ylo, YB * pair)
                for q in range(YB):
                    for k in range(KQ):
                        t = (q * KQ + k) * P
                        last = nc.tensor.matmul(y_ps[q][:, k, :], xs[s][:, t:t + P], cw[s][:, :],
                                                start=True, stop=True)
                    last.then_inc(s_y, 1)

            def stage2(pair, s, first, first_pair):
                pe.wait_ge(s_yhi, YB * (pair + 1))
                pe.wait_ge(s_ylo, YB * (pair + 1))
                if not (first and s < YS):
                    pe.wait_ge(s_res, HALVES * (pair - YS + 1))
                for h in range(HALVES):
                    for k in range(KT):
                        if first_pair and h == 0:
                            pe.wait_ge(s_w, k + 1)
                        for part in (y_hi, y_lo):
                            last = nc.tensor.matmul(z_ps[s % YS][h][:, :],
                                                    part[s % YS][:, k, :],
                                                    w[:, k, h * NH:(h + 1) * NH],
                                                    start=(k == 0 and part is y_hi),
                                                    stop=(k == KT - 1 and part is y_lo))
                    last.then_inc(s_z, 1)

            stage1(0, 0, 0, True)

            def body(r, first, last):
                for s in range(SLOTS):
                    pair = r * SLOTS + s
                    if not (last and s == SLOTS - 1):
                        stage1(pair + 1, (s + 1) % SLOTS, r + (s + 1) // SLOTS, False)
                    stage2(pair, s, first, first and s == 0)

            rounds(pe, body)


_INS = ['x', 'itok_B_0_15', 'L0_cond_weights', 'L0_ffn_w_q', 'L0_ffn_scale', 'L0_ffn_bias']
_OUTS = [((128, 64, 1024), 'float32')]


def kernel(**inputs):
    import numpy as _np
    import concourse.bacc as _bacc
    from concourse import mybir as _mybir
    from concourse.bass_utils import run_bass_kernel_spmd as _run

    nc = _bacc.Bacc("TRN2", target_bir_lowering=False, num_devices=1)
    arrays, args = {}, []
    for name in _INS:
        a = _np.ascontiguousarray(inputs[name])
        if a.dtype == _np.int8:
            a = a.view(_np.int32)
        arrays[f"in_{name}_dram"] = a
        args.append(nc.dram_tensor(f"in_{name}_dram", a.shape, _mybir.dt.from_np(a.dtype), kind="ExternalInput").ap())
    for i, (shape, dtype) in enumerate(_OUTS):
        dt = _mybir.dt.from_np(_np.dtype(dtype))
        args.append(nc.dram_tensor(f"out_{i}_dram", shape, dt, kind="ExternalOutput").ap())
    cond_ffn_residual(nc, *args)
    r = _run(nc, [arrays], core_ids=[0])
    got = tuple(r.results[0][f"out_{i}_dram"] for i in range(len(_OUTS)))
    return got[0]
```

```python
import concourse.bass as bass
from concourse import mybir
from contextlib import ExitStack


def cond_ffn_residual(
    nc: bass.Bass,
    x: bass.AP,
    cond: bass.AP,
    cond_w: bass.AP,
    w_q_words: bass.AP,
    scale: bass.AP,
    bias: bass.AP,
    out: bass.AP,
):
    fp32 = mybir.dt.float32
    fp32r = mybir.dt.float32r
    fp16 = mybir.dt.float16
    int8 = mybir.dt.int8
    int32 = mybir.dt.int32
    ALU = mybir.AluOpType
    ACT = mybir.ActivationFunctionType

    P = 128
    Q = 32
    NQ = P // Q
    B, C, T = x.shape
    _, S, D = cond_w.shape
    O = bias.shape[0]
    BP = P // C
    PAIRS = B // BP
    KT = T // P
    TQ = T // NQ
    NH = 512
    HALVES = O // NH
    SLOTS = 4
    ROUNDS = PAIRS // SLOTS
    TWO = 2
    GP = HALVES * BP
    DMA = 16
    WARM = 16
    WQ_FIRST = 3
    POOL_SCALES = [1]
    DVE_SCALES = [k for k in range(KT) if k not in POOL_SCALES]
    FIRST_HIGH = [2, 3]
    SECOND_TURN = 5
    FIRST_TURN = [0, 1]
    ACT_WIDENS = [3, 5]
    ACT_LAG = 1
    DVE_WIDENS = [k for k in range(KT) if k not in ACT_WIDENS]
    LAST = PAIRS - 1
    KH = KT // 2

    x_pairs = x.rearrange("(n b) c t -> n (b c) t", b=BP)
    out_pairs = out.rearrange("(n b) d o -> n (b d) o", b=BP)
    wq_tiles = w_q_words.rearrange("(g k t) o -> k g t o", g=NQ, t=Q)

    def rows(b):
        return slice(b * C, (b + 1) * C)

    def cols(h):
        return slice(h * NH, (h + 1) * NH)

    def exists(pair):
        return 0 <= pair < PAIRS if isinstance(pair, int) else True

    def at_least(eng, semaphore, value):
        if not isinstance(value, int) or value > 0:
            eng.wait_ge(semaphore, value)

    ctx = ExitStack()
    with ctx:
        def sb(name, shape, dt):
            return ctx.enter_context(nc.sbuf_tensor(name, shape, dt))

        def pb(name, shape, dt):
            return ctx.enter_context(nc.psum_tensor(name, shape, dt))

        def sem(name):
            return ctx.enter_context(nc.semaphore(name))

        cond_sb = sb("cond_sb", [1, B], int32)
        table = sb("table", [P, S, D], fp32)
        parts = sb("parts", [P, S, 3 * D], fp32r)
        wq_words = sb("wq_words", [P, KT, O // 4], int32)
        wq_sb = wq_words[:, :, :].bitcast(int8)
        wq16 = sb("wq16", [P, KT, O], fp16)
        w16 = sb("w16", [P, KT, O], fp16)
        w = sb("w", [P, KT, O], fp32r)
        scale_bc = sb("scale_bc", [P, O], fp16)
        bias_bc = sb("bias_bc", [P, O], fp16)
        table_load = sb("table_load", [P, 1], fp32)
        idle = sb("idle", [P, NH], fp16)
        xq = [sb(f"xq{s}", [P, NQ, TQ], fp32) for s in range(SLOTS)]
        xt = [sb(f"xt{s}", [P, KT, P], fp32) for s in range(TWO)]
        xt_hi = [sb(f"xt_hi{s}", [P, KT, P], fp32r) for s in range(TWO)]
        xt_lo = [sb(f"xt_lo{s}", [P, KT, P], fp32r) for s in range(TWO)]
        gg = [[sb(f"gg{s}_{b}", [P, O], fp32r) for b in range(BP)] for s in range(TWO)]
        cw = [[sb(f"cw{s}_{b}", [P, 2 * D], fp32r) for b in range(BP)] for s in range(TWO)]
        low = sb("low", [P, O], fp32)
        both = [sb(f"both{s}", [P, O], fp32) for s in range(TWO)]
        res = [sb(f"res{s}", [P, O], fp32) for s in range(SLOTS)]
        g_ps = [pb(f"g_ps{h}", [P, NH], fp32) for h in range(HALVES)]
        o_ps = [pb(f"o_ps{b}", [P, O], fp32) for b in range(BP)]

        s_cond = sem("cond_loaded")
        s_table = sem("table_loaded")
        s_scale = sem("scale_loaded")
        s_bias = sem("bias_loaded")
        s_wq = [sem(f"wq_loaded{k}") for k in range(KT)]
        s_wq16 = sem("wq16_ready")
        s_w16 = sem("w16_by_dve_ready")
        s_w16_pool = sem("w16_by_pool_ready")
        s_w_act = sem("w_by_act_ready")
        s_w_dve = sem("w_by_dve_ready")
        s_idle = sem("idle_zeroed")
        s_thi = sem("table_high_ready")
        s_tlo = sem("table_low_ready")
        s_xq = [sem(f"xq_loaded{s}") for s in range(SLOTS)]
        s_x = [sem(f"x_loaded{s}") for s in range(SLOTS)]
        s_first = {n: sem(f"first_pair_{n}") for n in ("xt", "xt_hi", "xt_lo")}
        s_xt = sem("xt_ready")
        s_xthi = sem("xt_hi_ready")
        s_xtlo = sem("xt_lo_ready")
        s_g = sem("g_half_done")
        s_ghi = sem("g_hi_ready")
        s_glo = sem("g_lo_ready")
        s_cw = sem("cw_ready")
        s_o = sem("o_batch_done")
        s_low = sem("low_ready")
        s_both = sem("both_ready")
        s_xb = sem("x_plus_bias_ready")
        s_res = sem("result_ready")
        s_last_o = sem("last_pair_o_done")
        s_last_sum = sem("last_pair_sum_ready")
        s_last_res = sem("last_pair_half_ready")
        s_last_out = sem("last_pair_half_stored")
        s_out = [sem(f"out_stored{s}") for s in range(SLOTS)]

        block = ctx.enter_context(nc.Block())

        def rounds(eng, period, extra):
            def one(r):
                for s in range(SLOTS):
                    period(r * SLOTS + s, s, r)

            one(0)
            with eng.Fori(1, ROUNDS - 1) as r:
                one(r)
            one(ROUNDS - 1)
            for s in range(extra):
                period(PAIRS + s, s, ROUNDS)

        @block.sync
        def _(sp):
            def pair_of(ap, pair):
                return ap[pair, :, :] if isinstance(pair, int) else (
                    ap[bass.ds(pair, 1), :, :].rearrange("a p t -> (a p) t"))

            def load_quarters(pair, s):
                for q in range(NQ):
                    sp.dma_start(xq[s][:, q, :],
                                 pair_of(x_pairs, pair)[q * Q:(q + 1) * Q, :].rearrange("c (g t) -> g c t", g=NQ)
                                 ).then_inc(s_xq[s], DMA)

            def load_x(pair, s):
                sp.dma_start(res[s][:, :], pair_of(x_pairs, pair)).then_inc(s_x[s], DMA)

            def load_wq(k):
                sp.dma_start(wq_words[:, k, :], wq_tiles[k, :, :, :]).then_inc(s_wq[k], DMA)

            sp.dma_start(scale_bc[:, :], scale.rearrange("(a o) -> a o", a=1).to_broadcast([P, O])
                         ).then_inc(s_scale, DMA)
            for k in range(WQ_FIRST):
                load_wq(k)
            load_quarters(0, 0)
            for k in range(WQ_FIRST, KT):
                load_wq(k)
            load_quarters(1, 1)
            sp.dma_start(cond_sb[:, :], cond.rearrange("(a b) -> a b", a=1)).then_inc(s_cond, DMA)
            for b in range(BP):
                sp.dma_start(table[rows(b), :, :], cond_w).then_inc(s_table, DMA)
            sp.dma_start(bias_bc[:, :], bias.rearrange("(a o) -> a o", a=1).to_broadcast([P, O])
                         ).then_inc(s_bias, DMA)
            load_x(0, 0)
            for s in range(2, SLOTS):
                load_quarters(s, s)

            def period(pair, s, r):
                if exists(pair + SLOTS):
                    sp.wait_ge(s_xt, pair + 1)
                    load_quarters(pair + SLOTS, s)
                if exists(pair + 1):
                    t = (s + 1) % SLOTS
                    at_least(sp, s_out[t], DMA * (r + (s + 1) // SLOTS))
                    load_x(pair + 1, t)
                if isinstance(pair, int) and pair - 2 == LAST:
                    sp.wait_ge(s_res, PAIRS)
                    sp.dma_start(out_pairs[LAST, :, cols(0)], res[LAST % SLOTS][:, cols(0)]).then_inc(s_last_out, DMA)
                    sp.wait_ge(s_last_res, BP)
                    sp.dma_start(out_pairs[LAST, :, cols(1)], res[LAST % SLOTS][:, cols(1)]).then_inc(s_last_out, DMA)
                elif exists(pair - 2):
                    t = (s - 2) % SLOTS
                    sp.wait_ge(s_res, pair - 1)
                    sp.dma_start(pair_of(out_pairs, pair - 2), res[t][:, :]).then_inc(s_out[t], DMA)

            rounds(sp, period, 2)
            for s in range(SLOTS):
                sp.wait_ge(s_out[s], DMA * (ROUNDS - (s == LAST % SLOTS)))
            sp.wait_ge(s_last_out, DMA * HALVES)

        @block.gpsimd
        def _(pool):
            def take_low(pair, two):
                pool.wait_ge(s_xt, pair + 1)
                pool.wait_ge(s_xthi, pair + 1)
                nc.gpsimd.tensor_tensor(xt_lo[two][:, :, :], xt[two][:, :, :], xt_hi[two][:, :, :].bitcast(fp32),
                                        ALU.subtract).then_inc(s_xtlo, 1)

            pool.wait_ge(s_scale, DMA)
            for k in POOL_SCALES:
                pool.wait_ge(s_wq16, k + 1)
                nc.gpsimd.tensor_tensor(w16[:, k, :], wq16[:, k, :], scale_bc[:, :], ALU.mult
                                        ).then_inc(s_w16_pool, 1)
            for n, ks in enumerate((slice(0, KH), slice(KH, KT))):
                pool.wait_ge(s_xthi if n else s_first["xt_hi"], 1)
                pool.wait_ge(s_xt if n else s_first["xt"], 1)
                nc.gpsimd.tensor_tensor(xt_lo[0][:, ks, :], xt[0][:, ks, :], xt_hi[0][:, ks, :].bitcast(fp32),
                                        ALU.subtract).then_inc(s_xtlo if n else s_first["xt_lo"], 1)

            def period(pair, s, r):
                if exists(pair - 2):
                    t = (s - 2) % SLOTS
                    pool.wait_ge(s_xb, pair - 1)
                    pool.wait_ge(s_both, BP * (pair - 1))
                    c = cols(0) if isinstance(pair, int) and pair - 2 == LAST else slice(0, O)
                    nc.gpsimd.tensor_tensor(res[t][:, c], res[t][:, c], both[s % TWO][:, c], ALU.add
                                            ).then_inc(s_res, 1)
                if exists(pair + 1):
                    at_least(pool, s_g, HALVES * pair)
                    take_low(pair + 1, (s + 1) % TWO)
                if exists(pair):
                    if isinstance(pair, int) and pair == 0:
                        pool.wait_ge(s_bias, DMA)
                    pool.wait_ge(s_x[s], DMA * (r + 1))
                    nc.gpsimd.tensor_tensor(res[s][:, :], res[s][:, :], bias_bc[:, :], ALU.add
                                            ).then_inc(s_xb, 1)

            rounds(pool, period, 2)

        @block.scalar
        def _(act):
            def take_high(pair, two):
                act.wait_ge(s_xt, pair + 1)
                nc.scalar.activation(xt_hi[two][:, :, :], xt[two][:, :, :], ACT.Copy).then_inc(s_xthi, 1)

            def pick(pair, two):
                for b in range(BP):
                    c = act.value_load(cond_sb[0:1, bass.ds(pair * BP + b, 1)], min_val=0, max_val=S - 1)
                    nc.scalar.activation(cw[two][b][:, :],
                                         parts[:, bass.ds(c, 1), b * D:(b + 2) * D].bitcast(fp32)
                                         .rearrange("p a d -> p (a d)"), ACT.Copy).then_inc(s_cw, 1)

            def g_high(pair, two, h):
                act.wait_ge(s_g, HALVES * pair + h + 1)
                for b in range(BP):
                    nc.scalar.activation(gg[two][b][rows(b), cols(h)], g_ps[h][rows(b), :], ACT.Copy
                                         ).then_inc(s_ghi, 1)

            act.wait_ge(s_idle, 1)
            nc.scalar.activation(table_load[:, :], idle[:, 0:1], ACT.Copy)
            for k in range(KT):
                act.wait_ge(s_wq[k], DMA)
                nc.scalar.activation(wq16[:, k, :], wq_sb[:, k, :], ACT.Copy).then_inc(s_wq16, 1)
                if k in FIRST_HIGH:
                    h = FIRST_HIGH.index(k)
                    ks = slice(h * KH, (h + 1) * KH)
                    act.wait_ge(s_xt if h else s_first["xt"], 1)
                    nc.scalar.activation(xt_hi[0][:, ks, :], xt[0][:, ks, :], ACT.Copy
                                         ).then_inc(s_xthi if h else s_first["xt_hi"], 1)
                if k - ACT_LAG in ACT_WIDENS:
                    act.wait_ge(s_w16, DVE_SCALES.index(k - ACT_LAG) + 1)
                    nc.scalar.activation(w[:, k - ACT_LAG, :], w16[:, k - ACT_LAG, :], ACT.Copy).then_inc(s_w_act, 1)

            def period(pair, s, r):
                if exists(pair - 1):
                    g_high(pair - 1, (s - 1) % TWO, 1)
                if exists(pair + 1):
                    at_least(act, s_g, HALVES * pair)
                    take_high(pair + 1, (s + 1) % TWO)
                if exists(pair):
                    at_least(act, s_o, BP * (pair - 1))
                    if isinstance(pair, int) and pair == 0:
                        act.wait_ge(s_table, BP * DMA)
                        for at in (0, 2 * D):
                            nc.scalar.activation(parts[:, :, at:at + D], table[:, :, :], ACT.Copy
                                                 ).then_inc(s_thi, 1)
                    g_high(pair, s % TWO, 0)
                    if isinstance(pair, int) and pair == 0:
                        act.wait_ge(s_thi, 2)
                        act.wait_ge(s_tlo, 1)
                        act.wait_ge(s_cond, DMA)
                    pick(pair, s % TWO)
                if isinstance(pair, int) and pair - 1 == LAST:
                    for b in range(BP):
                        act.wait_ge(s_last_o, b + 1)
                        act.wait_ge(s_both, BP * LAST)
                        nc.scalar.activation(low[rows(b), cols(0)], o_ps[b][rows(1 - b), cols(0)], ACT.Copy
                                             ).then_inc(s_low, 1)
                elif exists(pair - 1):
                    for b in range(BP):
                        act.wait_ge(s_o, BP * (pair - 1) + b + 1)
                        at_least(act, s_both, BP * (pair - 2) + b + 1)
                        nc.scalar.activation(low[rows(b), :], o_ps[b][rows(1 - b), :], ACT.Copy
                                             ).then_inc(s_low, 1)

            rounds(act, period, 1)

        @block.vector
        def _(dve):
            nc.vector.memset(idle[:, :], 0.0).then_inc(s_idle, 1)

            def transpose(pair, s, r, two):
                dve.wait_ge(s_xq[s], DMA * NQ * (r + 1))
                nc.vector.transpose(xt[two][:, :, :].rearrange("p j (q c) -> p q j c", c=Q),
                                    xq[s][:, :, :].rearrange("p q (j t) -> p q j t", t=Q)).then_inc(s_xt, 1)

            def g_low(pair, two, h):
                for b in range(BP):
                    dve.wait_ge(s_ghi, GP * pair + BP * h + b + 1)
                    nc.vector.tensor_tensor(gg[two][b][rows(1 - b), cols(h)], g_ps[h][rows(b), :],
                                            gg[two][b][rows(b), cols(h)].bitcast(fp32), ALU.subtract
                                            ).then_inc(s_glo, 1)

            dve.wait_ge(s_scale, DMA)
            for k in range(KT):
                if k in DVE_SCALES:
                    dve.wait_ge(s_wq16, k + 1)
                    nc.vector.tensor_tensor(w16[:, k, :], wq16[:, k, :], scale_bc[:, :], ALU.mult
                                            ).then_inc(s_w16, 1)
                if k in DVE_WIDENS:
                    if k in DVE_SCALES:
                        dve.wait_ge(s_w16, DVE_SCALES.index(k) + 1)
                    else:
                        dve.wait_ge(s_w16_pool, POOL_SCALES.index(k) + 1)
                    nc.vector.tensor_copy(w[:, k, :], w16[:, k, :]).then_inc(s_w_dve, 1)
                if k == SECOND_TURN:
                    transpose(1, 1, 0, 1)
                if k in FIRST_TURN:
                    h = FIRST_TURN.index(k)
                    dve.wait_ge(s_xq[0], DMA * NQ)
                    nc.vector.transpose(
                        xt[0][:, h * KH:(h + 1) * KH, :].rearrange("p j (q c) -> p q j c", c=Q),
                        xq[0][:, :, h * KH * Q:(h + 1) * KH * Q].rearrange("p q (j t) -> p q j t", t=Q)
                    ).then_inc(s_xt if h else s_first["xt"], 1)

            def period(pair, s, r):
                if exists(pair - 1):
                    g_low(pair - 1, (s - 1) % TWO, 1)
                if isinstance(pair, int) and pair == 0:
                    dve.wait_ge(s_thi, 1)
                    nc.vector.tensor_tensor(parts[:, :, D:2 * D], table[:, :, :], parts[:, :, 0:D].bitcast(fp32),
                                            ALU.subtract).then_inc(s_tlo, 1)
                if exists(pair + 2) and not (isinstance(pair, int) and pair == 0):
                    dve.wait_ge(s_xtlo, pair + 1)
                    transpose(pair + 2, (s + 2) % SLOTS, r + (s + 2) // SLOTS, s % TWO)
                if exists(pair):
                    g_low(pair, s % TWO, 0)
                if isinstance(pair, int) and pair == 0:
                    dve.wait_ge(s_xtlo, 1)
                    transpose(2, 2, 0, 0)
                if isinstance(pair, int) and pair - 1 == LAST:
                    at_least(dve, s_res, pair - 2)
                    for b in range(BP):
                        dve.wait_ge(s_last_o, b + 1)
                        dve.wait_ge(s_low, BP * LAST + b + 1)
                        nc.vector.tensor_tensor(both[LAST % TWO][rows(b), cols(0)], o_ps[b][rows(b), cols(0)],
                                                low[rows(b), cols(0)], ALU.add).then_inc(s_both, 1)
                    dve.wait_ge(s_xb, PAIRS)
                    end = res[LAST % SLOTS]
                    for b in range(BP):
                        dve.wait_ge(s_last_o, BP + b + 1)
                        nc.vector.tensor_tensor(end[rows(b), cols(1)], o_ps[b][rows(b), cols(1)],
                                                end[rows(b), cols(1)], ALU.add).then_inc(s_last_sum, 1)
                    for b in range(BP):
                        dve.wait_ge(s_last_sum, b + 1)
                        nc.vector.tensor_tensor(end[rows(b), cols(1)], o_ps[b][rows(1 - b), cols(1)],
                                                end[rows(b), cols(1)], ALU.add).then_inc(s_last_res, 1)
                elif exists(pair - 1):
                    at_least(dve, s_res, pair - 2)
                    for b in range(BP):
                        dve.wait_ge(s_o, BP * (pair - 1) + b + 1)
                        dve.wait_ge(s_low, BP * (pair - 1) + b + 1)
                        nc.vector.tensor_tensor(both[(s - 1) % TWO][rows(b), :], o_ps[b][rows(b), :],
                                                low[rows(b), :], ALU.add).then_inc(s_both, 1)

            rounds(dve, period, 1)

        @block.tensor
        def _(pe):
            def product(two, h, k):
                for part in (xt_hi, xt_lo):
                    last = nc.tensor.matmul(g_ps[h][:, :], part[two][:, k, :], w[:, k, cols(h)],
                                            start=(k == 0 and part is xt_hi),
                                            stop=(k == KT - 1 and part is xt_lo))
                if k == KT - 1:
                    last.then_inc(s_g, 1)

            def stage2(two, h):
                for k in range(KT):
                    product(two, h, k)

            def first_stage2():
                for k in range(KT):
                    if k in DVE_WIDENS:
                        pe.wait_ge(s_w_dve, DVE_WIDENS.index(k) + 1)
                    else:
                        pe.wait_ge(s_w_act, ACT_WIDENS.index(k) + 1)
                    if k % KH == 0:
                        pe.wait_ge(s_xthi if k else s_first["xt_hi"], 1)
                        pe.wait_ge(s_xtlo if k else s_first["xt_lo"], 1)
                    product(0, 0, k)
                    if k < KH:
                        product(0, 1, k)
                for k in range(KH, KT):
                    product(0, 1, k)

            def stage3_half(two, b, h):
                return nc.tensor.matmul(o_ps[b][:, cols(h)], cw[two][b][:, :], gg[two][b][:, cols(h)],
                                        start=True, stop=True)

            pe.wait_ge(s_idle, 1)
            for _ in range(WARM):
                nc.tensor.matmul(g_ps[0][:, :], idle[:, 0:P], idle[:, :], start=True, stop=True)

            def period(pair, s, r):
                if isinstance(pair, int) and pair == 0:
                    first_stage2()
                    return
                if isinstance(pair, int) and pair - 1 == LAST:
                    pe.wait_ge(s_cw, BP * PAIRS)
                    pe.wait_ge(s_both, BP * LAST)
                    for h in range(HALVES):
                        for b in range(BP):
                            pe.wait_ge(s_ghi, GP * LAST + BP * h + b + 1)
                            pe.wait_ge(s_glo, GP * LAST + BP * h + b + 1)
                            stage3_half(LAST % TWO, b, h).then_inc(s_last_o, 1)
                    return
                pe.wait_ge(s_xthi, pair + 1)
                pe.wait_ge(s_xtlo, pair + 1)
                pe.wait_ge(s_glo, GP * (pair - 1) + BP)
                stage2(s % TWO, 0)
                pe.wait_ge(s_ghi, GP * pair)
                pe.wait_ge(s_glo, GP * pair)
                pe.wait_ge(s_cw, BP * pair)
                at_least(pe, s_both, BP * (pair - 1))
                for b in range(BP):
                    for h in range(HALVES):
                        last = stage3_half((s - 1) % TWO, b, h)
                    last.then_inc(s_o, 1)
                stage2(s % TWO, 1)

            rounds(pe, period, 1)


_INS = ['x', 'itok_B_0_15', 'L0_cond_weights', 'L0_ffn_w_q', 'L0_ffn_scale', 'L0_ffn_bias']
_OUTS = [((128, 64, 1024), 'float32')]


def kernel(**inputs):
    import numpy as _np
    import concourse.bacc as _bacc
    from concourse import mybir as _mybir
    from concourse.bass_utils import run_bass_kernel_spmd as _run

    nc = _bacc.Bacc("TRN2", target_bir_lowering=False, num_devices=1)
    arrays, args = {}, []
    for name in _INS:
        a = _np.ascontiguousarray(inputs[name])
        if a.dtype == _np.int8:
            a = a.view(_np.int32)
        if name == 'L0_cond_weights':
            a = _np.ascontiguousarray(a.transpose(1, 0, 2))
        arrays[f"in_{name}_dram"] = a
        args.append(nc.dram_tensor(f"in_{name}_dram", a.shape, _mybir.dt.from_np(a.dtype), kind="ExternalInput").ap())
    for i, (shape, dtype) in enumerate(_OUTS):
        dt = _mybir.dt.from_np(_np.dtype(dtype))
        args.append(nc.dram_tensor(f"out_{i}_dram", shape, dt, kind="ExternalOutput").ap())
    cond_ffn_residual(nc, *args)
    r = _run(nc, [arrays], core_ids=[0])
    got = tuple(r.results[0][f"out_{i}_dram"] for i in range(len(_OUTS)))
    return got[0]
```
